# Optimizing a Trainium2 kernel written in Bass

```python
import numpy as np
import jax
import jax.numpy as jnp

def _softmax(x, axis=-1):
    return jax.nn.softmax(x, axis=axis)
def _gelu(x):
    return jax.nn.gelu(x, approximate=True)
def _silu(x):
    return jax.nn.silu(x)
def _sigmoid(x):
    return jax.nn.sigmoid(x)
def _layernorm(x, axis=-1, eps=1e-5):
    m = jnp.mean(x, axis=axis, keepdims=True)
    v = jnp.var(x, axis=axis, keepdims=True)
    return (x - m) / jnp.sqrt(v + eps)
def _scatter_add(tgt, idx, src, axis=0):
    return tgt.at[idx].add(src)
def _segment_sum(src, seg, n):
    return jax.ops.segment_sum(src, seg, n)

kernel_name = 'mk_conv_preact_d2_conv_nhwc16_8150a6'

def setup_inputs(seed: int = 0):
    np.random.seed(seed)
    _w = jnp.asarray
    def _rec_inputs():
        import jax
        import jax.numpy as jnp
        _gk = jax.random.key(seed)
        x = -7.109e-05 + 0.9999 * jax.random.normal(jax.random.fold_in(_gk, 1), (64, 256, 256, 16), jnp.float32)
        return x
    x = _rec_inputs()
    def _L0_conv_setup():
        import jax, jax.numpy as jnp
        import numpy as np
        from jax import lax
        N, H, W, C = (64, 256, 256, 16)
        O, K = (16, 3)
        key = jax.random.key(seed)
        k_in, k_u, k_v, k_w = jax.random.split(key, 4)
        u = jax.random.normal(k_u, (O, K), dtype=jnp.float32) * np.sqrt(2.0 / (O + K)).astype(np.float32)
        v = jax.random.normal(k_v, (O, K), dtype=jnp.float32) * np.sqrt(2.0 / (O + K)).astype(np.float32)
        w = jax.random.normal(k_w, (O, C), dtype=jnp.float32) * np.sqrt(2.0 / (O + C)).astype(np.float32)
        b = jnp.zeros((O,), dtype=jnp.float32)
        inputs = jax.random.normal(k_in, (N, H, W, C), dtype=jnp.float32)
        return {'inputs': inputs, 'u': u, 'v': v, 'w': w, 'b': b}
    _L0_conv_all = _L0_conv_setup()
    _L0_conv_in = {k: v for k, v in _L0_conv_all.items() if k in ('u', 'v', 'w', 'b', )}
    del _L0_conv_all

    def _L1_conv_setup():
        import jax, jax.numpy as jnp
        import numpy as np
        from jax import lax
        N, H, W, C = (64, 256, 256, 16)
        O, K = (16, 3)
        key = jax.random.key(seed)
        k_in, k_u, k_v, k_w = jax.random.split(key, 4)
        u = jax.random.normal(k_u, (O, K), dtype=jnp.float32) * np.sqrt(2.0 / (O + K)).astype(np.float32)
        v = jax.random.normal(k_v, (O, K), dtype=jnp.float32) * np.sqrt(2.0 / (O + K)).astype(np.float32)
        w = jax.random.normal(k_w, (O, C), dtype=jnp.float32) * np.sqrt(2.0 / (O + C)).astype(np.float32)
        b = jnp.zeros((O,), dtype=jnp.float32)
        inputs = jax.random.normal(k_in, (N, H, W, C), dtype=jnp.float32)
        return {'inputs': inputs, 'u': u, 'v': v, 'w': w, 'b': b}
    _L1_conv_all = _L1_conv_setup()
    _L1_conv_in = {k: v for k, v in _L1_conv_all.items() if k in ('u', 'v', 'w', 'b', )}
    del _L1_conv_all

    return {
        "x": x,
        "L0_conv_u": _L0_conv_in["u"],
        "L0_conv_v": _L0_conv_in["v"],
        "L0_conv_w": _L0_conv_in["w"],
        "L0_conv_b": _L0_conv_in["b"],
        "L1_conv_u": _L1_conv_in["u"],
        "L1_conv_v": _L1_conv_in["v"],
        "L1_conv_w": _L1_conv_in["w"],
        "L1_conv_b": _L1_conv_in["b"],
    }

def reference(x, L0_conv_u, L0_conv_v, L0_conv_w, L0_conv_b, L1_conv_u, L1_conv_v, L1_conv_w, L1_conv_b):
    import jax
    import jax.numpy as jnp
    def _L0_conv_ref(inputs, u, v, w, b):
        import jax, jax.numpy as jnp
        import numpy as np
        from jax import lax
        N, H, W, C = (64, 256, 256, 16)
        O, K = (16, 3)
        kern = jnp.einsum('lj,lk,li->ijkl', u, w, v)
        out = lax.conv_general_dilated(inputs, kern, window_strides=(1, 1), padding='SAME', dimension_numbers=('NHWC', 'HWIO', 'NHWC'))
        return jax.nn.relu(out + b)

    def _L1_conv_ref(inputs, u, v, w, b):
        import jax, jax.numpy as jnp
        import numpy as np
        from jax import lax
        N, H, W, C = (64, 256, 256, 16)
        O, K = (16, 3)
        kern = jnp.einsum('lj,lk,li->ijkl', u, w, v)
        out = lax.conv_general_dilated(inputs, kern, window_strides=(1, 1), padding='SAME', dimension_numbers=('NHWC', 'HWIO', 'NHWC'))
        return jax.nn.relu(out + b)

    def _gn(v, G=8, eps=1e-5):
        B_, H_, W_, C_ = v.shape
        g = v.reshape(B_, H_, W_, G, C_ // G)
        m = jnp.mean(g, axis=(1, 2, 4), keepdims=True)
        s = jnp.var(g, axis=(1, 2, 4), keepdims=True)
        return ((g - m) / jnp.sqrt(s + eps)).reshape(v.shape)

    def _ln_c(v, eps=1e-6):
        m = jnp.mean(v, axis=-1, keepdims=True)
        s = jnp.var(v, axis=-1, keepdims=True)
        return (v - m) / jnp.sqrt(s + eps)

    def _ln_t(v, eps=1e-5):
        m = jnp.mean(v, axis=-1, keepdims=True)
        s = jnp.var(v, axis=-1, keepdims=True)
        return (v - m) / jnp.sqrt(s + eps)

    def _to_tokens(v):
        B_, H_, W_, C_ = v.shape
        return v.reshape(B_, H_ * W_, C_)
    def _from_tokens(t, like):
        return t.reshape(like.shape)

    x = x + _L0_conv_ref(_gn(x), L0_conv_u, L0_conv_v, L0_conv_w, L0_conv_b)
    x = x + _L1_conv_ref(_gn(x), L1_conv_u, L1_conv_v, L1_conv_w, L1_conv_b)
    return x


_drawn_inputs = setup_inputs


def setup_inputs(seed=0):
    import zlib

    import numpy as np

    out = dict(_drawn_inputs(seed))
    spreads = {'L0_conv_b': (0.0, 0.1), 'L1_conv_b': (0.0, 0.1)}
    factors = {}
    for name, (base, spread) in spreads.items():
        noise = np.random.default_rng([zlib.crc32(name.encode()), seed]).standard_normal(out[name].shape)
        drawn = base * np.exp(spread * noise) if base else spread * noise
        out[name] = jnp.asarray(drawn.astype(out[name].dtype))
    for name, factor in factors.items():
        out[name] = (out[name] * factor).astype(out[name].dtype)
    return out
```

```python
from contextlib import ExitStack

import numpy as np

import concourse.bass as bass
from concourse import mybir

IMAGES, H, W, C = 64, 256, 256, 16
P = 128
HALVES = H // P
GN_GROUPS = 8
EPS = 1e-5
TAPS = 3
LAYERS = 2
PX = P // C
SPAN = PX + 2
BANK = 512
BUFS = 4
JOBS = BUFS * LAYERS
GROUPS = IMAGES // BUFS

TILES_W = []
_start = 0
while _start < W:
    _windows = [s for s in range(_start, _start + 4 * PX, PX) if s < W]
    _end = _windows[-1] + PX
    TILES_W.append((_start + (_start > 0), W - 1 if _end == W else _end - 2, _windows))
    _start = W if _end == W else _end - 2
TILES = [(half, *t) for half in range(HALVES) for t in TILES_W]
NT = len(TILES)

T_SLOTS = 3
PS_T, PS_Z, PS_B = 2, 2, 3
LOAD_AT = 6
STORE_AT = 3
EARLY = 2
SEAM_AT = 9
STAT_AT, ROOT_AT = 10, 12
BANDS = list(range(C))
BANDS.insert(SEAM_AT, "seam")
NB = len(BANDS)
ADD_PX = 32
ADDS = HALVES * W // ADD_PX
STATS = HALVES * GN_GROUPS
FILL_FROM = 3
FILL_A = 24
PARAMS = C + 2 * TAPS * C + C + TAPS + 1


def on_scalar(i):
    return i % 3 == 2


ZA = sum(on_scalar(i) for i in range(NT))
ZV = NT - ZA


def z_before(i, scalar):
    return sum(on_scalar(n) == scalar for n in range(i + 1))


def layer_of(k):
    return k % 4 // 2


def buf_of(k):
    return 2 * (k // 4) + k % 2


def build(nc, x, params, shifts, spans, seams, pick, out):
    fp32 = mybir.dt.float32
    ALU = mybir.AluOpType
    ACT = mybir.ActivationFunctionType
    AX = mybir.AxisListType

    x_rows = x.rearrange("n (s p) w c -> n p s (w c)", p=P)
    out_rows = out.rearrange("n (s p) w c -> n p s (w c)", p=P)

    with ExitStack() as ctx:
        def sb(name, shape):
            return ctx.enter_context(nc.sbuf_tensor(name, shape, fp32))

        def sem(name):
            return ctx.enter_context(nc.semaphore(name))

        X = [sb(f"image{b}", [P, HALVES, W * C]) for b in range(BUFS)]
        Z = sb("z", [P, C, HALVES, W])
        R = sb("relu", [P, C, HALVES, W])
        T = sb("transposed", [P, T_SLOTS, BANK])
        band = [sb(f"band{y}", [P, C, P]) for y in range(LAYERS)]
        mix = [sb(f"mix{y}", [P, SPAN, C]) for y in range(LAYERS)]
        seam_w = [sb(f"seam_w{y}", [P, P]) for y in range(LAYERS)]
        par = [sb(f"parameters{y}", [P, PARAMS]) for y in range(LAYERS)]
        shift = sb("shift", [P, TAPS, P])
        span = sb("span", [P, TAPS, SPAN])
        pick_s = sb("pick", [P, 2, GN_GROUPS])
        ones = sb("ones", [P, P])
        seam_z = sb("seam_z", [P, W])
        seam_r = sb("seam_r", [2 * C, W])
        bn = sb("bn", [P, STATS, 2, 3])
        squares = sb("squares", [P, STATS, 2])
        sums = sb("sums", [P, 2, GN_GROUPS])
        picked = sb("picked", [P, 2, GN_GROUPS])
        moments = sb("moments", [P, 2])
        small = sb("small", [P, 6])
        norm = sb("norm", [P, 2, 2])
        seam_mask = Z[:, 0:1, :, :].rearrange("p l s w -> p (l s w)")[:, 0:TAPS * P].rearrange(
            "p (i m) -> p i m", i=TAPS)
        z_flat = Z[:, 1:1 + LAYERS, :, :].rearrange("p l s w -> p l (s w)")
        mixed = [z_flat[:, y, 0:TAPS * C].rearrange("p (j l) -> p j l", j=TAPS) for y in range(LAYERS)]
        part = [z_flat[:, y, TAPS * C:(TAPS + SPAN) * C].rearrange("p (q l) -> p q l", q=SPAN)
                for y in range(LAYERS)]
        scratch = [R[:, 4 * y:4 * y + 4, :, :].rearrange("p l s w -> p (l s w)").rearrange(
            "p (l m) -> p l m", l=C) for y in range(LAYERS)]

        ps_t = [ctx.enter_context(nc.psum_tensor(f"ps_t{i}", [P, BANK], fp32)) for i in range(PS_T)]
        ps_z = [ctx.enter_context(nc.psum_tensor(f"ps_z{i}", [P, BANK], fp32)) for i in range(PS_Z)]
        ps_b = [ctx.enter_context(nc.psum_tensor(f"ps_b{i}", [P, BANK], fp32)) for i in range(PS_B)]
        ps_s = ctx.enter_context(nc.psum_tensor("ps_s", [P, BANK], fp32))

        const_in = sem("const_in")
        image_in = [sem(f"image_in{b}") for b in range(BUFS)]
        image_out = [sem(f"image_out{b}") for b in range(BUFS)]
        ones_set = sem("ones_set")
        built = sem("built")
        set_step = sem("set_step")
        set_step_pool = sem("set_step_pool")
        turned = sem("turned")
        normed = sem("normed")
        z_made = sem("z_made")
        z_vector = sem("z_vector")
        z_scalar = sem("z_scalar")
        seam_in = sem("seam_in")
        banded = sem("banded")
        relued = sem("relued")
        seam_out = sem("seam_out")
        added = sem("added")
        stat_step = sem("stat_step")
        stat_sums = sem("stat_sums")
        rooted = sem("rooted")
        norm_set = sem("norm_set")

        def value(per_job, t, k, count):
            return t * (JOBS * per_job) + (k * per_job + count)

        def grouped(eng, group):
            group(0, True, False)
            with eng.Fori(1, GROUPS - 1) as t:
                group(t, False, False)
            group(GROUPS - 1, False, True)

        block = ctx.enter_context(nc.Block())

        def build_matrices(engine, eng, y, steps):
            wt = par[y][:, 0:C]
            u = par[y][:, C:C + TAPS * C].rearrange("p (l j) -> p j l", j=TAPS)
            v = par[y][:, C + TAPS * C:C + 2 * TAPS * C].rearrange("p (l i) -> p i l", i=TAPS)
            seam_v = par[y][:, PARAMS - 1 - TAPS:PARAMS - 1]
            done = [0]

            def step(instruction):
                done[0] += 1
                instruction.then_inc(steps, 1)
                eng.wait_ge(steps, done[0])

            for j in range(TAPS):
                step(engine.tensor_tensor(mixed[y][:, j, :], wt, u[:, j, :], ALU.mult))
            shape = [P, SPAN, C]
            for j in range(TAPS):
                to = mix[y][:, :, :] if j == 0 else part[y]
                step(engine.tensor_tensor(to, span[:, j, :].unsqueeze(2).to_broadcast(shape),
                                          mixed[y][:, j, :].unsqueeze(1).to_broadcast(shape), ALU.mult))
                if j:
                    step(engine.tensor_tensor(mix[y][:], mix[y][:], part[y], ALU.add))
            shape = [P, C, P]
            for i in range(TAPS):
                to = band[y] if i == 0 else scratch[y]
                step(engine.tensor_tensor(to[:, :, :], shift[:, i, :].unsqueeze(1).to_broadcast(shape),
                                          v[:, i, :].unsqueeze(2).to_broadcast(shape), ALU.mult))
                if i:
                    step(engine.tensor_tensor(band[y][:], band[y][:], scratch[y][:, :, :], ALU.add))
            for i in range(TAPS):
                to = seam_w[y] if i == 0 else part[y].rearrange("p q l -> p (q l)")[:, 0:P]
                step(engine.tensor_tensor(to[:, :], seam_mask[:, i, :],
                                          seam_v[:, i:i + 1].to_broadcast([P, P]), ALU.mult))
                if i:
                    step(engine.tensor_tensor(seam_w[y][:], seam_w[y][:], to[:, :], ALU.add))
            engine.tensor_copy(small_done[y], par[y][:, 0:1]).then_inc(built, 1)

        small_done = [small[:, 4 + y:5 + y] for y in range(LAYERS)]

        @block.sync
        def _(sp):
            for y in range(LAYERS):
                sp.dma_start(par[y][:], params[y]).then_inc(const_in, 16)
            sp.dma_start(shift[:], shifts).then_inc(const_in, 16)
            sp.dma_start(span[:], spans).then_inc(const_in, 16)
            sp.dma_start(seam_mask, seams).then_inc(const_in, 16)
            sp.dma_start(pick_s[:], pick).then_inc(const_in, 16)
            for b in range(BUFS):
                sp.dma_start(X[b][:], x_rows[b]).then_inc(image_in[b], 16)

            def group(t, first, last):
                for k in range(JOBS):
                    sp.wait_ge(banded, value(NB, t, k, 1))
                    for s, p in enumerate((P - 2, 0)):
                        sp.dma_start(seam_z[2 * s * C:2 * (s + 1) * C, :],
                                     Z[p:p + 2, :, s, :]).then_inc(seam_in, 16)
                    sp.wait_ge(relued, value(NB, t, k, NB))
                    for r, (p, s) in enumerate(((P - 1, 0), (0, 1))):
                        sp.dma_start(R[p:p + 1, :, s, :], seam_r[r * C:(r + 1) * C, :]).then_inc(seam_out, 16)

            grouped(sp, group)

        @block.gpsimd
        def _(pool):
            nc.gpsimd.memset(ones[:], 1.0).then_inc(ones_set, 1)
            nc.gpsimd.memset(seam_z[:], 0.0).then_inc(ones_set, 1)
            pool.wait_ge(const_in, 16 * 6)
            build_matrices(nc.gpsimd, pool, 1, set_step_pool)

        @block.tensor
        def _(pe):
            def transposes(t, k, i):
                half, _, _, windows = TILES[i]
                b = buf_of(k)
                if layer_of(k) == 0:
                    pe.wait_ge(image_in[b], (t + 1) * 16)
                else:
                    chunks = (windows[-1] + PX - 1) // ADD_PX + 1
                    pe.wait_ge(added, value(ADDS, t, k - 2 + 1 - 1, half * (ADDS // HALVES) + chunks))
                if not (isinstance(t, int) and t == 0 and k == 0 and i < PS_T):
                    pe.wait_ge(normed, value(NT, t, k, i - PS_T + 1))
                for n, s in enumerate(windows):
                    last = nc.tensor.transpose(ps_t[i % PS_T][:, n * P:(n + 1) * P],
                                               X[b][:, half, s * C:(s + PX) * C], shift[:, 1, :])
                last.then_inc(turned, 1)

            def rows_step(t, k, i):
                _, lo, hi, windows = TILES[i]
                pe.wait_ge(normed, value(NT, t, k, i + 1))
                if i >= PS_Z:
                    scalar = on_scalar(i - PS_Z)
                    pe.wait_ge(z_scalar if scalar else z_vector,
                               value(ZA if scalar else ZV, t, k, z_before(i - PS_Z, scalar)))
                for n, s in enumerate(windows):
                    a, z = max(s - 1, lo), min(s + PX, hi)
                    last = nc.tensor.matmul(
                        ps_z[i % PS_Z][:, (a - lo) * C:(z + 1 - lo) * C],
                        T[:, i % T_SLOTS, n * P:(n + 1) * P],
                        mix[layer_of(k)][:, a - s + 1:z - s + 2, :].rearrange("p q l -> p (q l)"),
                        start=(n == 0), stop=(n == len(windows) - 1), skip_group_check=True)
                last.then_inc(z_made, 1)

            def group(t, first, last):
                for k in range(JOBS):
                    y = layer_of(k)
                    for i in range(NT):
                        if i < NT - PS_T:
                            transposes(t, k, i + PS_T)
                        rows_step(t, k, i)
                        if i >= NT - PS_T and k + 1 < JOBS:
                            transposes(t, k + 1, i + PS_T - NT)
                        elif i >= NT - PS_T and not last:
                            transposes(t + 1, 0, i + PS_T - NT)
                    pe.wait_ge(z_vector, value(ZV, t, k, ZV))
                    pe.wait_ge(z_scalar, value(ZA, t, k, ZA))
                    for m, l in enumerate(BANDS):
                        if m >= PS_B:
                            pe.wait_ge(relued, value(NB, t, k, m - PS_B + 1))
                        elif not (first and k == 0):
                            pe.wait_ge(relued, value(NB, t, k, -NB + (NB - 1 - m) // PS_B * PS_B + m + 1))
                        if l == "seam":
                            pe.wait_ge(seam_in, value(2 * 16, t, k, 2 * 16))
                            nc.tensor.matmul(ps_b[m % PS_B][:, 0:W], seam_w[y][:], seam_z[:],
                                             start=True, stop=True).then_inc(banded, 1)
                        else:
                            nc.tensor.matmul(ps_b[m % PS_B][:], band[y][:, l, :],
                                             Z[:, l, :, :].rearrange("p s w -> p (s w)"),
                                             start=True, stop=True).then_inc(banded, 1)
                        if m == STAT_AT and not (last and k == JOBS - 1):
                            stat_product(t, k + 1)

            def stat_product(t, k):
                pe.wait_ge(stat_step, value(STAT_STEPS, t, k, STAT_SUMS))
                nc.tensor.matmul(ps_s[:, 0:2 * GN_GROUPS], ones[:], sums[:].rearrange("p a g -> p (a g)"),
                                 start=True, stop=True).then_inc(stat_sums, 1)

            pe.wait_ge(const_in, 16 * 6)
            pe.wait_ge(ones_set, 2)
            for i in range(PS_T):
                transposes(0, 0, i)
            stat_product(0, 0)
            pe.wait_ge(built, LAYERS)
            grouped(pe, group)

        @block.scalar
        def _(act):
            def root(t, k):
                act.wait_ge(stat_step, value(STAT_STEPS, t, k, STAT_VAR))
                nc.scalar.activation(small[:, 2:3], small[:, 1:2], ACT.Sqrt).then_inc(rooted, 1)

            def normalise(t, k, i, first):
                n = len(TILES[i][3]) * P
                if i == 0:
                    act.wait_ge(norm_set, value(1, t, k, 1))
                act.wait_ge(turned, value(NT, t, k, i + 1))
                if not (first and k == 0 and i < T_SLOTS):
                    act.wait_ge(z_made, value(NT, t, k, i - T_SLOTS + 1))
                nc.scalar.activation(T[:, i % T_SLOTS, 0:n], ps_t[i % PS_T][:, 0:n], ACT.Identity,
                                     scale=norm[:, k % 2, 0:1], bias=norm[:, k % 2, 1:2]).then_inc(normed, 1)

            def store(t, b):
                act.dma_start(out_rows[t * BUFS + b], X[b][:]).then_inc(image_out[b], 16)

            def load(t, b):
                act.wait_ge(image_out[b], (t + 1) * 16)
                act.dma_start(X[b][:], x_rows[(t + 1) * BUFS + b]).then_inc(image_in[b], 16)

            def z_out(t, k, i):
                half, lo, hi, _ = TILES[i]
                act.wait_ge(z_made, value(NT, t, k, i + 1))
                nc.scalar.activation(
                    Z[:, :, half, lo:hi + 1],
                    ps_z[i % PS_Z][:, 0:(hi + 1 - lo) * C].rearrange("p (q l) -> p l q", l=C),
                    ACT.Identity).then_inc(z_scalar, 1)

            def group(t, first, last):
                for k in range(JOBS):
                    y = layer_of(k)
                    for i in range(NT):
                        if i >= EARLY or (first and k == 0):
                            normalise(t, k, i, first)
                        if i >= 2 and on_scalar(i - 2):
                            z_out(t, k, i - 2)
                        if i == LOAD_AT and layer_of(k - 2) == 1 and not (first and k < 2) and not (
                                last and k > 1):
                            load(t - 1 if k < 2 else t, buf_of((k - 2) % JOBS))
                    for i in range(NT - 2, NT):
                        if on_scalar(i):
                            z_out(t, k, i)
                    if not (first and k == 0):
                        act.wait_ge(added, value(ADDS, t, k, 0))
                    for m, l in enumerate(BANDS):
                        act.wait_ge(banded, value(NB, t, k, m + 1))
                        if l == "seam":
                            nc.scalar.activation(seam_r[:], ps_b[m % PS_B][0:2 * C, 0:W], ACT.Relu,
                                                 bias=par[y][0:2 * C, PARAMS - 1:PARAMS]).then_inc(relued, 1)
                        else:
                            at = C + 2 * TAPS * C + l
                            nc.scalar.activation(R[:, l, :, :].rearrange("p s w -> p (s w)"),
                                                 ps_b[m % PS_B][:], ACT.Relu,
                                                 bias=par[y][:, at:at + 1]).then_inc(relued, 1)
                        if m == STORE_AT and layer_of(k - 1) == 1 and not (first and k == 0):
                            store(t - 1 if k == 0 else t, buf_of((k - 1) % JOBS))
                        if m == ROOT_AT and not (last and k == JOBS - 1):
                            root(t, k + 1)
                        if m >= NB - 1 - EARLY and m < NB - 1 and not (last and k == JOBS - 1):
                            normalise(t, k + 1, m - (NB - 1 - EARLY), False)

            act.wait_ge(const_in, 16 * 6)
            root(0, 0)
            grouped(act, group)
            act.wait_ge(added, IMAGES * LAYERS * ADDS)
            store(GROUPS - 1, BUFS - 1)
            for b in range(BUFS):
                act.wait_ge(image_out[b], GROUPS * 16)

        @block.vector
        def _(dve):
            def z_out(t, k, i):
                half, lo, hi, _ = TILES[i]
                dve.wait_ge(z_made, value(NT, t, k, i + 1))
                nc.vector.tensor_copy(
                    Z[:, :, half, lo:hi + 1],
                    ps_z[i % PS_Z][:, 0:(hi + 1 - lo) * C].rearrange("p (q l) -> p l q", l=C),
                ).then_inc(z_vector, 1)

            def add(t, k, c):
                s, w0 = c // (ADDS // HALVES), c % (ADDS // HALVES) * ADD_PX
                if c == 0:
                    dve.wait_ge(seam_out, value(2 * 16, t, k, 2 * 16))
                x_px = X[buf_of(k % JOBS)][:, s, w0 * C:(w0 + ADD_PX) * C].rearrange("p (w c) -> p w c", c=C)
                nc.vector.tensor_tensor(x_px, x_px, R[:, :, s, w0:w0 + ADD_PX].rearrange("p c w -> p w c"),
                                        ALU.add).then_inc(added, 1)

            def stat(t, k, n):
                if n == 0:
                    if layer_of(k) == 0:
                        dve.wait_ge(image_in[buf_of(k % JOBS)], (t + k // JOBS + 1) * 16)
                    else:
                        dve.wait_ge(added, value(ADDS, t, k - 1, 0))
                g, s = n % GN_GROUPS, n // GN_GROUPS
                pair = X[buf_of(k % JOBS)][:, s, :].rearrange("p (w c) -> p w c", c=C)[:, :, 2 * g:2 * g + 2]
                return nc.vector.bn_stats(bn[:, n, :, :].rearrange("p a b -> p (a b)"), pair)

            def norm_of(t, k, last_stat):
                done = [0]

                def step(instruction):
                    done[0] += 1
                    instruction.then_inc(stat_step, 1)
                    dve.wait_ge(stat_step, value(STAT_STEPS, t, k, done[0]))

                per = float(P * HALVES * W * 2 // (P * HALVES * 2))
                means, m2s = bn[:, :, :, 1], bn[:, :, :, 2]
                step(last_stat)
                step(nc.vector.tensor_tensor(squares[:], means, means, ALU.mult))
                step(nc.vector.scalar_tensor_tensor(out=squares[:], in0=squares[:], scalar=per, in1=m2s,
                                                    op0=ALU.mult, op1=ALU.add))
                step(nc.vector.tensor_reduce(sums[:, 0, :], bn[:, :, :, 1].rearrange(
                    "p (s g) a -> p g s a", s=HALVES), AX.XY, ALU.add))
                step(nc.vector.tensor_reduce(sums[:, 1, :], squares[:].rearrange(
                    "p (s g) a -> p g s a", s=HALVES), AX.XY, ALU.add))
                assert done[0] == STAT_SUMS
                dve.wait_ge(stat_sums, value(1, t, k, 1))
                step(nc.vector.tensor_tensor(picked[:].rearrange("p a g -> p (a g)"), ps_s[:, 0:2 * GN_GROUPS],
                                             pick_s[:].rearrange("p a g -> p (a g)"), ALU.mult))
                step(nc.vector.tensor_reduce(moments[:], picked[:], AX.X, ALU.add))
                mean, square = moments[:, 0:1], moments[:, 1:2]
                step(nc.vector.tensor_tensor(small[:, 0:1], mean, mean, ALU.mult))
                step(nc.vector.tensor_scalar(small[:, 3:4], square, small[:, 0:1], EPS,
                                             ALU.subtract, ALU.add))
                step(nc.vector.reciprocal(small[:, 1:2], small[:, 3:4]))
                assert done[0] == STAT_VAR
                dve.wait_ge(rooted, value(1, t, k, 1))
                scale, bias = norm[:, k % 2, 0:1], norm[:, k % 2, 1:2]
                step(nc.vector.tensor_scalar(small[:, 0:1], small[:, 2:3], small[:, 2:3], small[:, 3:4],
                                             ALU.mult, ALU.mult))
                step(nc.vector.tensor_scalar(small[:, 0:1], small[:, 0:1], -0.5, 1.5, ALU.mult, ALU.add))
                step(nc.vector.tensor_tensor(scale, small[:, 0:1], small[:, 2:3], ALU.mult))
                nc.vector.tensor_scalar(bias, mean, scale, -1.0, ALU.mult, ALU.mult).then_inc(norm_set, 1)
                assert done[0] == STAT_STEPS

            def group(t, first, last):
                for k in range(JOBS):
                    fill = []
                    if not (first and k == 0):
                        fill += [("add", c) for c in range(ADDS)]
                    if not (last and k == JOBS - 1):
                        fill += [("stat", n) for n in range(STATS)]

                    early = min(FILL_A, len(fill) - 1)

                    def do(count):
                        for what, n in fill[:count]:
                            if what == "add":
                                add(t, k - 1, n)
                            else:
                                ins = stat(t, k + 1, n)
                                if n == STATS - 1:
                                    norm_of(t, k + 1, ins)
                        del fill[:count]

                    for i in range(NT):
                        if not on_scalar(i):
                            z_out(t, k, i)
                        if i >= FILL_FROM:
                            do(early * (i + 1 - FILL_FROM) // (NT - FILL_FROM)
                               - early * (i - FILL_FROM) // (NT - FILL_FROM))
                    do(len(fill))

            dve.wait_ge(const_in, 16 * 6)
            for n in range(STATS):
                ins = stat(0, 0, n)
            norm_of(0, 0, ins)
            build_matrices(nc.vector, dve, 0, set_step)
            grouped(dve, group)
            for c in range(ADDS):
                add(GROUPS - 1, JOBS - 1, c)


STAT_SUMS, STAT_VAR, STAT_STEPS = 5, 10, 13


def constants():
    row, col = np.arange(P)[:, None], np.arange(P)[None, :]
    shifts = np.stack([row == col + i - 1 for i in range(TAPS)], 1).astype(np.float32)
    px, slot = np.arange(P)[:, None] // C, np.arange(SPAN)[None, :]
    spans = np.stack([px - slot + 2 == j for j in range(TAPS)], 1).astype(np.float32)
    same = (row % C == col % C) & (row < 4 * C) & (col < 2 * C)
    seams = np.stack([same & (row // C - col // C == i) for i in range(TAPS)], 1).astype(np.float32)
    group = (np.arange(P) % C // (C // GN_GROUPS))[:, None] == np.arange(GN_GROUPS)[None, :]
    pick = np.stack([group / (P * HALVES * 2), group / (P * HALVES * 2 * W)], 1).astype(np.float32)
    return {"shifts": shifts, "spans": spans, "seams": seams, "pick": pick}


def layer_params(u, v, w, b):
    def row(a):
        return np.tile(a.reshape(1, -1), (P, 1))
    return np.concatenate([np.tile(w.T, (PX, 1)), row(u), row(v), row(b),
                           np.tile(v, (P // C, 1)), np.tile(b[:, None], (P // C, 1))], axis=1)


def kernel(x, L0_conv_u, L0_conv_v, L0_conv_w, L0_conv_b, L1_conv_u, L1_conv_v, L1_conv_w, L1_conv_b):
    import concourse.bacc as bacc
    from concourse.bass_utils import run_bass_kernel_spmd

    layers = [[np.asarray(a) for a in q] for q in (
        (L0_conv_u, L0_conv_v, L0_conv_w, L0_conv_b), (L1_conv_u, L1_conv_v, L1_conv_w, L1_conv_b))]
    arrays = {"x": np.ascontiguousarray(x),
              "params": np.ascontiguousarray(np.stack([layer_params(*q) for q in layers])), **constants()}
    nc = bacc.Bacc("TRN2", target_bir_lowering=False, num_devices=1, dynamic_dma_scratch_size=1024)
    aps = {n: nc.dram_tensor("in_" + n, a.shape, mybir.dt.from_np(a.dtype), kind="ExternalInput").ap()
           for n, a in arrays.items()}
    out = nc.dram_tensor("out", (IMAGES, H, W, C), mybir.dt.float32, kind="ExternalOutput").ap()
    build(nc, aps["x"], aps["params"], aps["shifts"], aps["spans"], aps["seams"], aps["pick"], out)
    result = run_bass_kernel_spmd(nc, [{"in_" + n: a for n, a in arrays.items()}], core_ids=[0])
    return result.results[0]["out"]
```
